# Optimizing a Trainium2 kernel written in Bass

```python
import numpy as np
import jax
import jax.numpy as jnp

def _softmax(x, axis=-1):
    return jax.nn.softmax(x, axis=axis)

def _gelu(x):
    return jax.nn.gelu(x, approximate=True)

def _silu(x):
    return jax.nn.silu(x)

def _sigmoid(x):
    return jax.nn.sigmoid(x)

def _layernorm(x, axis=-1, eps=1e-05):
    m = jnp.mean(x, axis=axis, keepdims=True)
    v = jnp.var(x, axis=axis, keepdims=True)
    return (x - m) / jnp.sqrt(v + eps)

def _scatter_add(tgt, idx, src, axis=0):
    return tgt.at[idx].add(src)

def _segment_sum(src, seg, n):
    return jax.ops.segment_sum(src, seg, n)
kernel_name = 'mk_rec_standalone_d1_rec_r8_3043a9'

def setup_inputs(seed: int=0):
    np.random.seed(seed)
    _w = jnp.asarray

    def _rec_inputs():
        import jax
        import jax.numpy as jnp
        _rk = jax.random.key(seed)
        r_user_rep = -0.000928989 + 1.00043 * jax.random.normal(jax.random.fold_in(_rk, 1), (1024, 512), jnp.float32)
        r_indices = jnp.stack([jax.random.randint(jax.random.fold_in(jax.random.fold_in(_rk, 2), 0), (1024,), 55, 99965, jnp.int32), jax.random.randint(jax.random.fold_in(jax.random.fold_in(_rk, 2), 1), (1024,), 48, 12496, jnp.int32), jax.random.randint(jax.random.fold_in(jax.random.fold_in(_rk, 2), 2), (1024,), 45, 99915, jnp.int32), jax.random.randint(jax.random.fold_in(jax.random.fold_in(_rk, 2), 3), (1024,), 60, 99946, jnp.int32), jax.random.randint(jax.random.fold_in(jax.random.fold_in(_rk, 2), 4), (1024,), 7, 99948, jnp.int32), jax.random.randint(jax.random.fold_in(jax.random.fold_in(_rk, 2), 5), (1024,), 33, 99999, jnp.int32), jax.random.randint(jax.random.fold_in(jax.random.fold_in(_rk, 2), 6), (1024,), 75, 99987, jnp.int32), jax.random.randint(jax.random.fold_in(jax.random.fold_in(_rk, 2), 7), (1024,), 20, 99950, jnp.int32), jax.random.randint(jax.random.fold_in(jax.random.fold_in(_rk, 2), 8), (1024,), 14, 99970, jnp.int32), jax.random.randint(jax.random.fold_in(jax.random.fold_in(_rk, 2), 9), (1024,), 36, 99989, jnp.int32), jax.random.randint(jax.random.fold_in(jax.random.fold_in(_rk, 2), 10), (1024,), 4, 99993, jnp.int32), jax.random.randint(jax.random.fold_in(jax.random.fold_in(_rk, 2), 11), (1024,), 56, 99973, jnp.int32), jax.random.randint(jax.random.fold_in(jax.random.fold_in(_rk, 2), 12), (1024,), 15, 99974, jnp.int32), jax.random.randint(jax.random.fold_in(jax.random.fold_in(_rk, 2), 13), (1024,), 97, 99986, jnp.int32), jax.random.randint(jax.random.fold_in(jax.random.fold_in(_rk, 2), 14), (1024,), 23, 99998, jnp.int32), jax.random.randint(jax.random.fold_in(jax.random.fold_in(_rk, 2), 15), (1024,), 57, 99994, jnp.int32), jax.random.randint(jax.random.fold_in(jax.random.fold_in(_rk, 2), 16), (1024,), 6, 12495, jnp.int32), jax.random.randint(jax.random.fold_in(jax.random.fold_in(_rk, 2), 17), (1024,), 1, 12469, jnp.int32), jax.random.randint(jax.random.fold_in(jax.random.fold_in(_rk, 2), 18), (1024,), 24, 99879, jnp.int32), jax.random.randint(jax.random.fold_in(jax.random.fold_in(_rk, 2), 19), (1024,), 200, 99973, jnp.int32), jax.random.randint(jax.random.fold_in(jax.random.fold_in(_rk, 2), 20), (1024,), 89, 12495, jnp.int32), jax.random.randint(jax.random.fold_in(jax.random.fold_in(_rk, 2), 21), (1024,), 68, 99881, jnp.int32), jax.random.randint(jax.random.fold_in(jax.random.fold_in(_rk, 2), 22), (1024,), 2, 99901, jnp.int32), jax.random.randint(jax.random.fold_in(jax.random.fold_in(_rk, 2), 23), (1024,), 74, 12479, jnp.int32), jax.random.randint(jax.random.fold_in(jax.random.fold_in(_rk, 2), 24), (1024,), 53, 99950, jnp.int32), jax.random.randint(jax.random.fold_in(jax.random.fold_in(_rk, 2), 25), (1024,), 69, 99982, jnp.int32), jax.random.randint(jax.random.fold_in(jax.random.fold_in(_rk, 2), 26), (1024,), 175, 99910, jnp.int32), jax.random.randint(jax.random.fold_in(jax.random.fold_in(_rk, 2), 27), (1024,), 135, 99953, jnp.int32), jax.random.randint(jax.random.fold_in(jax.random.fold_in(_rk, 2), 28), (1024,), 19, 99994, jnp.int32), jax.random.randint(jax.random.fold_in(jax.random.fold_in(_rk, 2), 29), (1024,), 122, 99955, jnp.int32), jax.random.randint(jax.random.fold_in(jax.random.fold_in(_rk, 2), 30), (1024,), 8, 99927, jnp.int32), jax.random.randint(jax.random.fold_in(jax.random.fold_in(_rk, 2), 31), (1024,), 13, 99979, jnp.int32), jax.random.randint(jax.random.fold_in(jax.random.fold_in(_rk, 2), 32), (1024,), 120, 99930, jnp.int32), jax.random.randint(jax.random.fold_in(jax.random.fold_in(_rk, 2), 33), (1024,), 5, 99972, jnp.int32), jax.random.randint(jax.random.fold_in(jax.random.fold_in(_rk, 2), 34), (1024,), 81, 99879, jnp.int32), jax.random.randint(jax.random.fold_in(jax.random.fold_in(_rk, 2), 35), (1024,), 2, 99958, jnp.int32), jax.random.randint(jax.random.fold_in(jax.random.fold_in(_rk, 2), 36), (1024,), 2, 99998, jnp.int32), jax.random.randint(jax.random.fold_in(jax.random.fold_in(_rk, 2), 37), (1024,), 57, 99983, jnp.int32), jax.random.randint(jax.random.fold_in(jax.random.fold_in(_rk, 2), 38), (1024,), 63, 99987, jnp.int32), jax.random.randint(jax.random.fold_in(jax.random.fold_in(_rk, 2), 39), (1024,), 35, 99956, jnp.int32), jax.random.randint(jax.random.fold_in(jax.random.fold_in(_rk, 2), 40), (1024,), 1, 12490, jnp.int32), jax.random.randint(jax.random.fold_in(jax.random.fold_in(_rk, 2), 41), (1024,), 27, 99969, jnp.int32), jax.random.randint(jax.random.fold_in(jax.random.fold_in(_rk, 2), 42), (1024,), 0, 12495, jnp.int32), jax.random.randint(jax.random.fold_in(jax.random.fold_in(_rk, 2), 43), (1024,), 25, 99926, jnp.int32), jax.random.randint(jax.random.fold_in(jax.random.fold_in(_rk, 2), 44), (1024,), 28, 99839, jnp.int32), jax.random.randint(jax.random.fold_in(jax.random.fold_in(_rk, 2), 45), (1024,), 5, 99986, jnp.int32), jax.random.randint(jax.random.fold_in(jax.random.fold_in(_rk, 2), 46), (1024,), 20, 99986, jnp.int32), jax.random.randint(jax.random.fold_in(jax.random.fold_in(_rk, 2), 47), (1024,), 4, 99981, jnp.int32), jax.random.randint(jax.random.fold_in(jax.random.fold_in(_rk, 2), 48), (1024,), 55, 99954, jnp.int32), jax.random.randint(jax.random.fold_in(jax.random.fold_in(_rk, 2), 49), (1024,), 21, 99978, jnp.int32)], axis=1)
        return (r_user_rep, r_indices)
    r_user_rep, r_indices = _rec_inputs()

    def _L0_rec_setup():
        import jax, jax.numpy as jnp
        import numpy as np
        key = jax.random.key(seed)
        ks = jax.random.split(key, 6)
        B, K, V, H = (256, 50, 12500, 512)
        return {'user_rep': jax.random.normal(ks[0], (B, H), dtype=jnp.float32), 'indices': jax.random.randint(ks[1], (B, K), 0, V, dtype=jnp.int64), 'item_embeddings': jax.random.normal(ks[2], (V, H), dtype=jnp.float32), 'W_fuse': jax.random.normal(ks[3], (2 * H, H), dtype=jnp.float32) * (1.0 / np.sqrt(2 * H)), 'b_fuse': jnp.zeros((H,), dtype=jnp.float32), 'W_proj': jax.random.normal(ks[4], (H, V), dtype=jnp.float32) * (1.0 / np.sqrt(H)), 'b_proj': jnp.zeros((V,), dtype=jnp.float32)}
    _L0_rec_all = _L0_rec_setup()
    _L0_rec_in = {k: v for k, v in _L0_rec_all.items() if k in ('item_embeddings', 'W_fuse', 'b_fuse', 'W_proj', 'b_proj')}
    del _L0_rec_all
    return {'r_user_rep': r_user_rep, 'r_indices': r_indices, 'L0_rec_item_embeddings': _L0_rec_in['item_embeddings'], 'L0_rec_W_fuse': _L0_rec_in['W_fuse'], 'L0_rec_b_fuse': _L0_rec_in['b_fuse'], 'L0_rec_W_proj': _L0_rec_in['W_proj'], 'L0_rec_b_proj': _L0_rec_in['b_proj']}

def reference(r_user_rep, r_indices, L0_rec_item_embeddings, L0_rec_W_fuse, L0_rec_b_fuse, L0_rec_W_proj, L0_rec_b_proj):
    import jax
    import jax.numpy as jnp

    def _L0_rec_ref(user_rep, indices, item_embeddings, W_fuse, b_fuse, W_proj, b_proj):
        import jax, jax.numpy as jnp
        import numpy as np
        retrieved = jnp.mean(item_embeddings[indices], axis=1)
        fused_input = jnp.concatenate([user_rep, retrieved], axis=1)
        fused_rep = fused_input @ W_fuse + b_fuse
        logits = fused_rep @ W_proj + b_proj
        return logits
    y = _L0_rec_ref(r_user_rep, r_indices, L0_rec_item_embeddings, L0_rec_W_fuse, L0_rec_b_fuse, L0_rec_W_proj, L0_rec_b_proj)
    return y

_drawn_inputs = setup_inputs


def setup_inputs(seed=0):
    import zlib

    import numpy as np

    out = dict(_drawn_inputs(seed))
    spreads = {'L0_rec_b_fuse': (0.0, 0.1), 'L0_rec_b_proj': (0.0, 0.1)}
    factors = {}
    for name, (base, spread) in spreads.items():
        noise = np.random.default_rng([zlib.crc32(name.encode()), seed]).standard_normal(out[name].shape)
        drawn = base * np.exp(spread * noise) if base else spread * noise
        out[name] = jnp.asarray(drawn.astype(out[name].dtype))
    for name, factor in factors.items():
        out[name] = (out[name] * factor).astype(out[name].dtype)
    return out
```

```python
import concourse.bass as bass
from concourse import mybir
from contextlib import ExitStack

P = 128
USERS, BAG, H, V = 1024, 50, 512, 12500
BLOCKS = USERS // P
KT = H // P
CHUNK = 500
CHUNKS = V // CHUNK
SLOTS = 5
ROUNDS = CHUNKS // SLOTS
GROUP = (3, 5)
BANKS = 5
FAST = 24
RING = 8
LAST = V - 1
ACCS = 2
SUM_STEPS = 2 + FAST + 1
AHEAD = 2
REPLACED = -1.0e9


def program(nc, user_t, indices, items, w_fuse, b_fuse, w_proj, b_proj, out):
    f32, f32r, i32 = mybir.dt.float32, mybir.dt.float32r, mybir.dt.int32
    ALU, ACT, AX = mybir.AluOpType, mybir.ActivationFunctionType, mybir.AxisListType

    w_view = w_proj.rearrange("(t p) n -> p t n", p=P)
    ctx = ExitStack()
    with ctx:
        def sb(name, shape, dt=f32):
            return ctx.enter_context(nc.sbuf_tensor(name, shape, dt))

        def sem(name):
            return ctx.enter_context(nc.semaphore(name))

        chunk_bytes, fused_bytes = KT * CHUNK * 4, KT * USERS * 4
        arena = sb("arena", [P, (SLOTS * chunk_bytes + fused_bytes) // 4])
        at = nc.lookup_mloc(arena).addr
        w_raw = nc.alloc_sbuf_tensor_at("w_raw", [P, SLOTS, KT, CHUNK], f32, offset=at)
        w_lo = nc.alloc_sbuf_tensor_at("w_lo", [P, SLOTS, KT, CHUNK], f32r, offset=at)
        user_part = nc.alloc_sbuf_tensor_at("user_part", [P, KT, USERS], f32, offset=at + SLOTS * chunk_bytes)
        fused_lo = nc.alloc_sbuf_tensor_at("fused_lo", [P, KT, USERS], f32r, offset=at + SLOTS * chunk_bytes)
        w_hi = sb("w_hi", [P, SLOTS, KT, CHUNK], f32r)
        fused_hi = sb("fused_hi", [P, KT, USERS], f32r)
        bias = sb("bias", [P, SLOTS, CHUNK])
        stage = sb("stage", [P, BANKS, CHUNK])
        rows = sb("rows", [P, RING, H])
        spill_row = sb("spill_row", [P, H])
        acc = sb("acc", [P, ACCS, H])
        bag = sb("bag", [P, H])
        mean_t = sb("mean_t", [P, H])
        fused = sb("fused", [P, KT, P])
        wf = sb("wf", [P, 2 * KT, H])
        bf = sb("bf", [P, KT])
        ut = sb("ut", [P, KT, USERS])
        last_row = sb("last_row", [P, H])
        raw_index = sb("raw_index", [P, BLOCKS, BAG], i32)
        wrap = sb("wrap", [P, BLOCKS, BAG])
        key = sb("key", [P, BLOCKS, BAG])
        top = sb("top", [P, BLOCKS, FAST])
        index = sb("index", [P, BLOCKS, FAST], i32)
        mask = sb("mask", [P, BLOCKS, FAST])
        rest_index = sb("rest_index", [P, BLOCKS, BAG], i32)
        rest_mask = sb("rest_mask", [P, BLOCKS, BAG])
        n_last = sb("n_last", [P, BLOCKS])
        now_index = sb("now_index", [P, 2, FAST], i32)
        now_mask = sb("now_mask", [P, FAST])
        spill_index = sb("spill_index", [P, 1], i32)
        spill_mask = sb("spill_mask", [P, 1])
        rest_max = sb("rest_max", [P, 1])
        rest_any = sb("rest_any", [P, 1])
        ones = sb("ones", [P, 1])
        spills = sb("spills", [1, 1], i32)
        ident = sb("ident", [P, P])

        bank = [ctx.enter_context(nc.psum_tensor(f"bank{n}", [P, 512], f32)) for n in range(8)]
        ps_mean, ps_fused, ps_flag = bank[BANKS], bank[BANKS + 1], bank[BANKS + 2]

        index_in, last_in, weights_in = sem("index_in"), sem("last_in"), sem("weights_in")
        w_in = [sem(f"w_in{s}") for s in range(SLOTS)]
        w_hi_done, w_lo_done = sem("w_hi_done"), sem("w_lo_done")
        row_in = [sem(f"row_in{r}") for r in range(RING)]
        vec_step = sem("vec_step")
        zeroed, ident_done, ones_done = sem("zeroed"), sem("ident_done"), sem("ones_done")
        index_now = sem("index_now")
        rest_flagged, flag_summed, flag_ready = sem("rest_flagged"), sem("flag_summed"), sem("flag_ready")
        asked, store_asked = sem("asked"), sem("store_asked")
        spill_closed = sem("spill_closed")
        spill_named, spill_in, spill_added = sem("spill_named"), sem("spill_in"), sem("spill_added")
        user_done, user_kept = sem("user_done"), sem("user_kept")
        bag_turned, mean_ready = sem("bag_turned"), sem("mean_ready")
        fuse_done, fused_ready, fused_hi_done, fused_lo_done = (
            sem("fuse_done"), sem("fused_ready"), sem("fused_hi_done"), sem("fused_lo_done"))
        unit_done = sem("unit_done")
        evacuated = [sem(f"evacuated{k}") for k in range(BANKS)]
        stored = [sem(f"stored{k}") for k in range(BANKS)]

        def flat(t):
            return t[:, :, :].rearrange("p b k -> p (b k)")

        def units(j, g):
            first = sum(GROUP[:g])
            for m in range(GROUP[g]):
                u = j * GROUP[g] + m
                yield first + m, u

        def uses(i, u, g):
            return (SLOTS * GROUP[0] * ROUNDS // BANKS if g else 0) + i * (SLOTS * GROUP[g] // BANKS) + u // BANKS

        def unit_number(i, u, g):
            return (SLOTS * GROUP[0] * ROUNDS if g else 0) + i * (SLOTS * GROUP[g]) + u

        block = ctx.enter_context(nc.Block())

        @block.sync
        def _(sp):
            sp.dma_start(raw_index[:, :, :], indices.rearrange("(b p) k -> p b k", p=P)).then_inc(index_in, 16)
            sp.dma_start(last_row[:, :], items[LAST:V, :].to_broadcast([P, H])).then_inc(last_in, 16)
            sp.dma_start(wf[:, :, :], w_fuse.rearrange("(t p) n -> p t n", p=P)).then_inc(weights_in, 16)
            sp.dma_start(ut[:, :, :], user_t.rearrange("(t p) n -> p t n", p=P)).then_inc(weights_in, 16)
            with nc.allow_non_contiguous_dma(reason="512 biases, once"):
                sp.dma_start(bf[:, :], b_fuse.rearrange("(t p) -> p t", p=P)).then_inc(weights_in, 16)

            def load(slot, chunk_start):
                sp.dma_start(w_raw[:, slot, :, :], w_view[:, :, bass.ds(chunk_start, CHUNK)]).then_inc(w_in[slot], 16)
                sp.dma_start(bias[:, slot, :],
                             b_proj[:, bass.ds(chunk_start, CHUNK)].to_broadcast([P, CHUNK])).then_inc(w_in[slot], 16)

            def store(i, j, g):
                for b, u in units(j, g):
                    k = u % BANKS
                    sp.wait_ge(evacuated[k], uses(i, u, g) + 1)
                    sp.sem_inc(store_asked, 1)
                    sp.dma_start(out[b * P:(b + 1) * P, bass.ds(i * (SLOTS * CHUNK) + j * CHUNK, CHUNK)],
                                 stage[:, k, :]).then_inc(stored[k], 16)

            def body(i, g, then):
                for j in range(SLOTS):
                    slot = (j + SLOTS - 1) % SLOTS
                    if j == 0:
                        load(slot, i * (SLOTS * CHUNK) + slot * CHUNK)
                    elif then is not None:
                        load(slot, then * (SLOTS * CHUNK) + slot * CHUNK)
                    store(i, j, g)

            for slot in range(SLOTS - 1):
                load(slot, slot * CHUNK)
            with sp.Fori(0, ROUNDS - 1) as i:
                body(i, 0, i + 1)
            body(ROUNDS - 1, 0, 0)
            with sp.Fori(0, ROUNDS - 1) as i:
                body(i, 1, i + 1)
            body(ROUNDS - 1, 1, None)
            for k in range(BANKS):
                sp.wait_ge(stored[k], 16 * (BLOCKS * CHUNKS // BANKS))

        @block.gpsimd
        def _(pool):
            pool.memset(ident[:, :], 0.0).then_inc(zeroed, 1)
            pool.memset(ones[:, :], 1.0).then_inc(ones_done, 1)
            pool.wait_ge(zeroed, 1)
            pool.affine_select(out=ident[:, :], in_=ident[:, :], compare_op=ALU.not_equal, fill=1.0,
                               base=0, pattern=[[-1, P]], channel_multiplier=1).then_inc(ident_done, 1)

            bound = pool.to_reg(LAST - 1)

            def fetch(into, entry, done):
                pool.sem_inc(asked, 1)
                pool.indirect_dma_start(into, None, items, bass.IndirectOffsetOnAxis(entry, 0),
                                        bounds_check=bound, oob_is_err=False).then_inc(done, 16)

            def fetch_block(b, half):
                pool.tensor_copy(now_index[:, half, :], flat(index)[:, bass.ds(b * FAST, FAST)]).then_inc(index_now, 1)
                pool.wait_ge(index_now, b + 1)
                for j in range(FAST):
                    if j < RING:
                        pool.wait_ge(vec_step, SORT_STEPS + b * SUM_STEPS - RING + j)
                    else:
                        pool.wait_ge(vec_step, SORT_STEPS + b * SUM_STEPS + 2 + j - RING + 1)
                    fetch(rows[:, j % RING, :], now_index[:, half, j:j + 1], row_in[j % RING])
                pool.wait_ge(flag_ready, 1)
                spill = pool.value_load(spills[0:1, 0:1], min_val=0, max_val=1)
                with pool.If(spill):
                    with pool.Fori(0, BAG) as c:
                        pool.wait_ge(spill_named, b * BAG + c + 1)
                        fetch(spill_row[:, :], spill_index[:, 0:1], spill_in)

            pool.wait_ge(vec_step, SORT_STEPS)
            with pool.Fori(0, BLOCKS // 2) as i:
                fetch_block(2 * i, 0)
                fetch_block(2 * i + 1, 1)

        @block.scalar
        def _(act):
            def split_hi(slot, use):
                act.wait_ge(w_in[slot], 32 * (use + 1))
                nc.scalar.activation(w_hi[:, slot, :, :], w_raw[:, slot, :, :], ACT.Copy).then_inc(w_hi_done, 1)

            def fuse(b):
                act.wait_ge(bag_turned, b + 1)
                nc.scalar.activation(mean_t[:, :], ps_mean[:, :], ACT.Copy, scale=1.0 / BAG).then_inc(mean_ready, 1)
                act.wait_ge(fused_ready, b + 1)
                nc.scalar.activation(fused_hi[:, :, bass.ds(b * P, P)], fused[:, :, :], ACT.Copy).then_inc(fused_hi_done, 1)

            act.wait_ge(weights_in, 48)
            for t in range(KT):
                for half in range(2):
                    n = 2 * t + half
                    act.wait_ge(user_done, n + 1)
                    nc.scalar.activation(user_part[:, t, half * 512:half * 512 + 512], bank[n][:, :], ACT.Identity,
                                         bias=bf[:, t:t + 1]).then_inc(user_kept, 1)
            for slot in range(AHEAD):
                split_hi(slot, 0)
            with act.Fori(0, GROUP[0]) as b:
                fuse(b)

            def body(i, g, ahead=SLOTS):
                for j in range(ahead):
                    slot = (j + AHEAD) % SLOTS
                    split_hi(slot, i + g * ROUNDS + (j + AHEAD) // SLOTS)
                if g == 0:
                    fuse(i + GROUP[0])

            with act.Fori(0, ROUNDS) as i:
                body(i, 0)
            with act.Fori(0, ROUNDS - 1) as i:
                body(i, 1)
            body(ROUNDS - 1, 1, SLOTS - AHEAD)

        @block.tensor
        def _(pe):
            pe.wait_ge(weights_in, 48)
            for t in range(KT):
                for half in range(2):
                    n = 2 * t + half
                    for k in range(KT):
                        mm = nc.tensor.matmul(bank[n][:, :], wf[:, k, t * P:(t + 1) * P],
                                              ut[:, k, half * 512:half * 512 + 512], start=k == 0, stop=k == KT - 1)
                    mm.then_inc(user_done, 1)
            pe.wait_ge(user_kept, 2 * KT)
            pe.wait_ge(rest_flagged, 1)
            pe.wait_ge(ones_done, 1)
            nc.tensor.matmul(ps_flag[0:1, 0:1], rest_any[:, :], ones[:, :], start=True, stop=True).then_inc(flag_summed, 1)
            pe.wait_ge(ident_done, 1)

            def turn_bag(b):
                pe.wait_ge(vec_step, SORT_STEPS + (b + 1) * SUM_STEPS)
                pe.wait_ge(mean_ready, b)
                for t in range(KT):
                    mm = nc.tensor.transpose(ps_mean[:, t * P:(t + 1) * P], bag[:, t * P:(t + 1) * P], ident[:, :])
                mm.then_inc(bag_turned, 1)

            def fuse(b):
                pe.wait_ge(mean_ready, b + 1)
                pe.wait_ge(fused_ready, b)
                for t in range(KT):
                    for k in range(KT):
                        mm = nc.tensor.matmul(ps_fused[:, t * P:(t + 1) * P], wf[:, KT + k, t * P:(t + 1) * P],
                                              mean_t[:, k * P:(k + 1) * P], start=k == 0, stop=k == KT - 1)
                mm.then_inc(fuse_done, 1)

            with pe.Fori(0, GROUP[0]) as b:
                turn_bag(b)
                fuse(b)

            def unit(i, j, b, u, g):
                k = u % BANKS
                pe.wait_ge(evacuated[k], uses(i, u, g))
                for t in range(KT):
                    hi, lo = fused_hi[:, t, b * P:(b + 1) * P], fused_lo[:, t, b * P:(b + 1) * P]
                    nc.tensor.matmul(bank[k][:, 0:CHUNK], hi, w_hi[:, j, t, :], start=t == 0, stop=False)
                    nc.tensor.matmul(bank[k][:, 0:CHUNK], hi, w_lo[:, j, t, :], start=False, stop=False)
                    mm = nc.tensor.matmul(bank[k][:, 0:CHUNK], lo, w_hi[:, j, t, :], start=False, stop=t == KT - 1)
                return mm

            def body(i, g):
                for j in range(SLOTS):
                    pe.wait_ge(w_lo_done, (i + g * ROUNDS) * SLOTS + j + 1)
                    last_chunk = g == 0 and j == SLOTS - 1
                    if last_chunk:
                        turn_bag(i + GROUP[0])
                    for b, u in units(j, g):
                        unit(i, j, b, u, g).then_inc(unit_done, 1)
                        if last_chunk and b == 0:
                            fuse(i + GROUP[0])

            pe.wait_ge(fused_lo_done, GROUP[0])
            with pe.Fori(0, ROUNDS) as i:
                body(i, 0)
            pe.wait_ge(fused_lo_done, BLOCKS)
            with pe.Fori(0, ROUNDS) as i:
                body(i, 1)

        @block.vector
        def _(dve):
            steps = [0]

            def step(instruction):
                steps[0] += 1
                instruction.then_inc(vec_step, 1)
                return steps[0]

            v = nc.vector
            step(v.memset(rows[:, :, :], 0.0))
            step(v.memset(spill_row[:, :], 0.0))
            dve.wait_ge(index_in, 16)
            n = step(v.tensor_scalar(wrap[:, :, :], raw_index[:, :, :], 0.0, float(V), ALU.is_lt, ALU.mult))
            dve.wait_ge(vec_step, n)
            n = step(v.tensor_tensor(key[:, :, :], raw_index[:, :, :], wrap[:, :, :], ALU.add))
            dve.wait_ge(vec_step, n)
            n = step(v.tensor_scalar(key[:, :, :], key[:, :, :], 0.0, float(LAST), ALU.max, ALU.min))
            dve.wait_ge(vec_step, n)
            n = step(v.tensor_scalar(key[:, :, :], key[:, :, :], -1.0, None, ALU.mult))
            dve.wait_ge(vec_step, n)
            n = step(v.tensor_scalar(wrap[:, :, :], key[:, :, :], -float(LAST), None, ALU.is_equal))
            dve.wait_ge(vec_step, n)
            step(v.tensor_reduce(n_last[:, :], wrap[:, :, :], AX.X, ALU.add))
            for e in range(0, FAST, 8):
                for b in range(BLOCKS):
                    n = step(v.max(top[:, b, e:e + 8], key[:, b, :]))
                dve.wait_ge(vec_step, n)
                for b in range(BLOCKS):
                    n = step(v.match_replace(key[:, b, :], top[:, b, e:e + 8], key[:, b, :], REPLACED))
                dve.wait_ge(vec_step, n)
            step(v.tensor_scalar(index[:, :, :], top[:, :, :], -1.0, None, ALU.mult))
            step(v.tensor_scalar(mask[:, :, :], top[:, :, :], -float(LAST), None, ALU.is_gt))
            step(v.tensor_scalar(rest_index[:, :, :], key[:, :, :], -1.0, None, ALU.mult))
            n = step(v.tensor_scalar(rest_mask[:, :, :], key[:, :, :], -float(LAST), None, ALU.is_gt))
            dve.wait_ge(vec_step, n)
            assert steps[0] == SORT_STEPS
            v.tensor_reduce(rest_any[:, :], rest_mask[:, :, :], AX.XY, ALU.max).then_inc(rest_flagged, 1)
            dve.wait_ge(flag_summed, 1)
            v.tensor_scalar(spills[0:1, 0:1], ps_flag[0:1, 0:1], 1.0, None, ALU.min).then_inc(flag_ready, 1)
            dve.wait_ge(flag_ready, 1)
            spill = dve.value_load(spills[0:1, 0:1], min_val=0, max_val=1)

            def sum_start(b):
                done = SORT_STEPS + b * SUM_STEPS
                dve.wait_ge(vec_step, done)
                v.tensor_copy(now_mask[:, :], flat(mask)[:, bass.ds(b * FAST, FAST)]).then_inc(vec_step, 1)
                v.tensor_scalar(acc[:, 0, :], last_row[:, :], n_last[:, bass.ds(b, 1)], None, ALU.mult).then_inc(vec_step, 1)

            def add_row(b, j):
                done = SORT_STEPS + b * SUM_STEPS + 2
                dve.wait_ge(vec_step, done + max(0, j - 1))
                dve.wait_ge(row_in[j % RING], 16 * (b * (FAST // RING) + j // RING + 1))
                part, row, m = acc[:, j % ACCS, :], rows[:, j % RING, :], now_mask[:, j:j + 1]
                if j == 1:
                    v.tensor_scalar(part, row, m, None, ALU.mult).then_inc(vec_step, 1)
                else:
                    v.scalar_tensor_tensor(part, row, m, part, ALU.mult, ALU.add).then_inc(vec_step, 1)

            def sum_end(b):
                done = SORT_STEPS + b * SUM_STEPS + 2 + FAST
                with dve.If(spill):
                    with dve.Fori(0, BAG) as c:
                        dve.wait_ge(vec_step, done)
                        dve.wait_ge(spill_added, 3 * (b * BAG + c))
                        v.tensor_copy(spill_mask[:, :], flat(rest_mask)[:, bass.ds(b * BAG + c, 1)]).then_inc(spill_added, 1)
                        v.tensor_copy(spill_index[:, :], flat(rest_index)[:, bass.ds(b * BAG + c, 1)]).then_inc(spill_named, 1)
                        dve.wait_ge(spill_in, 16 * (b * BAG + c + 1))
                        dve.wait_ge(spill_added, 3 * (b * BAG + c) + 1)
                        v.scalar_tensor_tensor(acc[:, 0, :], spill_row[:, :], spill_mask[:, :], acc[:, 0, :],
                                               ALU.mult, ALU.add).then_inc(spill_added, 2)
                    dve.wait_ge(spill_added, 3 * (b + 1) * BAG)
                    dve.sem_inc(spill_closed, 1)
                dve.wait_ge(vec_step, done)
                dve.wait_ge(bag_turned, b)
                v.tensor_tensor(bag[:, :], acc[:, 0, :], acc[:, 1, :], ALU.add).then_inc(vec_step, 1)

            def fuse_add(b):
                dve.wait_ge(fuse_done, b + 1)
                dve.wait_ge(fused_hi_done, b)
                dve.wait_ge(fused_lo_done, b)
                v.tensor_tensor(fused[:, :, :], ps_fused[:, :].rearrange("p (t u) -> p t u", t=KT),
                                user_part[:, :, bass.ds(b * P, P)], ALU.add).then_inc(fused_ready, 1)

            def fuse_lo(b):
                dve.wait_ge(fused_hi_done, b + 1)
                dve.wait_ge(fused_ready, b + 1)
                v.tensor_tensor(fused_lo[:, :, bass.ds(b * P, P)], fused[:, :, :],
                                fused_hi[:, :, bass.ds(b * P, P)].bitcast(f32), ALU.subtract).then_inc(fused_lo_done, 1)

            def split_lo(i, slot):
                dve.wait_ge(w_hi_done, i * SLOTS + slot + 1)
                v.tensor_tensor(w_lo[:, slot, :, :], w_raw[:, slot, :, :],
                                w_hi[:, slot, :, :].bitcast(f32), ALU.subtract).then_inc(w_lo_done, 1)

            def evacuate(i, j, u, g):
                k = u % BANKS
                dve.wait_ge(unit_done, unit_number(i, u, g) + 1)
                dve.wait_ge(stored[k], 16 * uses(i, u, g))
                v.tensor_tensor(stage[:, k, :], bank[k][:, 0:CHUNK], bias[:, j, :], ALU.add).then_inc(evacuated[k], 1)

            dve.wait_ge(last_in, 16)
            dve.wait_ge(user_kept, 2 * KT)
            for slot in range(AHEAD):
                split_lo(0, slot)
            with dve.Fori(0, GROUP[0]) as b:
                sum_start(b)
                for j in range(FAST):
                    add_row(b, j)
                sum_end(b)
                fuse_add(b)
                fuse_lo(b)

            def body(i, g, ahead=SLOTS):
                b = i + GROUP[0]
                for j in range(SLOTS):
                    if j < ahead:
                        split_lo(i + g * ROUNDS + (j + AHEAD) // SLOTS, (j + AHEAD) % SLOTS)
                    if g == 0 and j < SLOTS - 1:
                        per = FAST // (SLOTS - 1)
                        if j == 0:
                            sum_start(b)
                        for r in range(j * per, (j + 1) * per):
                            add_row(b, r)
                        if j == SLOTS - 2:
                            sum_end(b)
                    for m, (_, u) in enumerate(units(j, g)):
                        evacuate(i, j, u, g)
                        if g == 0 and j == SLOTS - 1 and m == 1:
                            fuse_add(b)
                    if g == 0 and j == SLOTS - 1:
                        fuse_lo(b)

            with dve.Fori(0, ROUNDS) as i:
                body(i, 0)
            with dve.Fori(0, ROUNDS - 1) as i:
                body(i, 1)
            body(ROUNDS - 1, 1, SLOTS - AHEAD)


SORT_STEPS = 2 + 6 + FAST // 8 * 2 * BLOCKS + 4


def kernel(r_user_rep, r_indices, L0_rec_item_embeddings, L0_rec_W_fuse, L0_rec_b_fuse, L0_rec_W_proj, L0_rec_b_proj):
    import numpy as np
    import concourse.bacc as bacc
    from concourse.bass_utils import run_bass_kernel_spmd

    nc = bacc.Bacc("TRN2", target_bir_lowering=False, num_devices=1)
    given = {
        "user_t": np.ascontiguousarray(np.asarray(r_user_rep).T),
        "indices": np.ascontiguousarray(r_indices),
        "items": np.ascontiguousarray(L0_rec_item_embeddings),
        "w_fuse": np.ascontiguousarray(L0_rec_W_fuse),
        "b_fuse": np.ascontiguousarray(L0_rec_b_fuse),
        "w_proj": np.ascontiguousarray(L0_rec_W_proj),
        "b_proj": np.ascontiguousarray(L0_rec_b_proj).reshape(1, V),
    }
    args = [nc.dram_tensor(name, a.shape, mybir.dt.from_np(a.dtype), kind="ExternalInput").ap()
            for name, a in given.items()]
    out = nc.dram_tensor("out", (USERS, V), mybir.dt.float32, kind="ExternalOutput").ap()
    program(nc, *args, out)
    got = run_bass_kernel_spmd(nc, [given], core_ids=[0])
    return got.results[0]["out"]
```

```python
import concourse.bass as bass
from concourse import mybir
from contextlib import ExitStack

P = 128
USERS, BAG, H, V = 1024, 50, 512, 12500
BLOCKS = USERS // P
KT = H // P
CHUNK = 500
CHUNKS = V // CHUNK
SLOTS = 5
ROUNDS = CHUNKS // SLOTS
GROUP = BLOCKS // 2
BANKS = 5
FAST = 24
RING = 8
LAST = V - 1
ACCS = 2
SUM_STEPS = 2 + FAST + 1
AHEAD = 2
REPLACED = -1.0e9


def program(nc, user_t, indices, items, w_fuse, b_fuse, w_proj, b_proj, out):
    f32, f32r, i32 = mybir.dt.float32, mybir.dt.float32r, mybir.dt.int32
    ALU, ACT, AX = mybir.AluOpType, mybir.ActivationFunctionType, mybir.AxisListType

    w_view = w_proj.rearrange("(t p) n -> p t n", p=P)
    ctx = ExitStack()
    with ctx:
        def sb(name, shape, dt=f32):
            return ctx.enter_context(nc.sbuf_tensor(name, shape, dt))

        def sem(name):
            return ctx.enter_context(nc.semaphore(name))

        chunk_bytes, fused_bytes = KT * CHUNK * 4, KT * USERS * 4
        arena = sb("arena", [P, (SLOTS * chunk_bytes + fused_bytes) // 4])
        at = nc.lookup_mloc(arena).addr
        w_raw = nc.alloc_sbuf_tensor_at("w_raw", [P, SLOTS, KT, CHUNK], f32, offset=at)
        w_lo = nc.alloc_sbuf_tensor_at("w_lo", [P, SLOTS, KT, CHUNK], f32r, offset=at)
        user_part = nc.alloc_sbuf_tensor_at("user_part", [P, KT, USERS], f32, offset=at + SLOTS * chunk_bytes)
        fused_lo = nc.alloc_sbuf_tensor_at("fused_lo", [P, KT, USERS], f32r, offset=at + SLOTS * chunk_bytes)
        w_hi = sb("w_hi", [P, SLOTS, KT, CHUNK], f32r)
        fused_hi = sb("fused_hi", [P, KT, USERS], f32r)
        bias = sb("bias", [P, SLOTS, CHUNK])
        stage = sb("stage", [P, BANKS, CHUNK])
        rows = sb("rows", [P, RING, H])
        spill_row = sb("spill_row", [P, H])
        acc = sb("acc", [P, ACCS, H])
        bag = sb("bag", [P, H])
        mean_t = sb("mean_t", [P, H])
        fused = sb("fused", [P, KT, P])
        wf = sb("wf", [P, 2 * KT, H])
        bf = sb("bf", [P, KT])
        ut = sb("ut", [P, KT, USERS])
        last_row = sb("last_row", [P, H])
        raw_index = sb("raw_index", [P, BLOCKS, BAG], i32)
        wrap = sb("wrap", [P, BLOCKS, BAG])
        key = sb("key", [P, BLOCKS, BAG])
        top = sb("top", [P, BLOCKS, FAST])
        index = sb("index", [P, BLOCKS, FAST], i32)
        mask = sb("mask", [P, BLOCKS, FAST])
        rest_index = sb("rest_index", [P, BLOCKS, BAG], i32)
        rest_mask = sb("rest_mask", [P, BLOCKS, BAG])
        n_last = sb("n_last", [P, BLOCKS])
        now_index = sb("now_index", [P, 2, FAST], i32)
        now_mask = sb("now_mask", [P, FAST])
        spill_index = sb("spill_index", [P, 1], i32)
        spill_mask = sb("spill_mask", [P, 1])
        rest_max = sb("rest_max", [P, 1])
        rest_any = sb("rest_any", [P, 1])
        ones = sb("ones", [P, 1])
        spills = sb("spills", [1, 1], i32)
        ident = sb("ident", [P, P])

        bank = [ctx.enter_context(nc.psum_tensor(f"bank{n}", [P, 512], f32)) for n in range(8)]
        ps_mean, ps_fused, ps_flag = bank[BANKS], bank[BANKS + 1], bank[BANKS + 2]

        index_in, last_in = sem("index_in"), sem("last_in")
        wf_user_in, wf_item_in = sem("wf_user_in"), sem("wf_item_in")
        users_in = [sem("users_in0"), sem("users_in1")]
        w_in = [sem(f"w_in{s}") for s in range(SLOTS)]
        w_hi_done, w_lo_done = sem("w_hi_done"), sem("w_lo_done")
        row_in = [sem(f"row_in{r}") for r in range(RING)]
        sort_step, sorted_blocks = sem("sort_step"), sem("sorted_blocks")
        sum_step = sem("sum_step")
        ident_zeroed, ident_done, ones_done = sem("ident_zeroed"), sem("ident_done"), sem("ones_done")
        rows_zeroed, index_now = sem("rows_zeroed"), sem("index_now")
        rest_flagged, flag_summed, flag_ready = sem("rest_flagged"), sem("flag_summed"), sem("flag_ready")
        fetch_asked, store_asked, spill_closed = sem("fetch_asked"), sem("store_asked"), sem("spill_closed")
        spill_named, spill_in, spill_added = sem("spill_named"), sem("spill_in"), sem("spill_added")
        user_done, user_kept = sem("user_done"), sem("user_kept")
        bag_turned, mean_ready = sem("bag_turned"), sem("mean_ready")
        fuse_done, fused_ready, fused_hi_done, fused_lo_done = (
            sem("fuse_done"), sem("fused_ready"), sem("fused_hi_done"), sem("fused_lo_done"))
        unit_done = sem("unit_done")
        evacuated = [sem(f"evacuated{k}") for k in range(BANKS)]
        stored = [sem(f"stored{k}") for k in range(BANKS)]

        per_round = SLOTS * GROUP

        def units(j, g):
            return [(g * GROUP + m, j * GROUP + m) for m in range(GROUP)]

        def number(i, u, g):
            return (g * ROUNDS + i) * per_round + u

        def uses(i, u, g):
            return (g * ROUNDS + i) * (per_round // BANKS) + u // BANKS

        def flat(t):
            return t[:, :, :].rearrange("p b k -> p (b k)")

        block = ctx.enter_context(nc.Block())

        @block.sync
        def _(sp):
            def load(slot, chunk_start):
                sp.dma_start(w_raw[:, slot, :, :], w_view[:, :, bass.ds(chunk_start, CHUNK)]).then_inc(w_in[slot], 16)
                sp.dma_start(bias[:, slot, :],
                             b_proj[:, bass.ds(chunk_start, CHUNK)].to_broadcast([P, CHUNK])).then_inc(w_in[slot], 16)

            def load_users(half):
                sp.dma_start(ut[:, :, half * 512:half * 512 + 512],
                             user_t.rearrange("(t p) n -> p t n", p=P)[:, :, half * 512:half * 512 + 512]
                             ).then_inc(users_in[half], 16)

            def store(b, chunk_start, k):
                sp.dma_start(out[b * P:(b + 1) * P, bass.ds(chunk_start, CHUNK)], stage[:, k, :]).then_inc(stored[k], 16)

            sp.dma_start(raw_index[:, :, :], indices.rearrange("(b p) k -> p b k", p=P)).then_inc(index_in, 16)
            wf_view = w_fuse.rearrange("(t p) n -> p t n", p=P)
            sp.dma_start(wf[:, 0:KT, :], wf_view[:, 0:KT, :]).then_inc(wf_user_in, 16)
            load_users(0)
            sp.dma_start(last_row[:, :], items[LAST:V, :].to_broadcast([P, H])).then_inc(last_in, 16)
            with nc.allow_non_contiguous_dma(reason="512 biases, once"):
                sp.dma_start(bf[:, :], b_fuse.rearrange("(t p) -> p t", p=P)).then_inc(wf_user_in, 16)
            sp.dma_start(wf[:, KT:2 * KT, :], wf_view[:, KT:2 * KT, :]).then_inc(wf_item_in, 16)
            for slot in range(SLOTS):
                load(slot, slot * CHUNK)
                if slot == 1:
                    load_users(1)

            for b in range(GROUP):
                for j in range(SLOTS):
                    sp.wait_ge(evacuated[j], b + 1)
                    store(b, j * CHUNK, j)
                    if b == GROUP - 1 and j < SLOTS - 1:
                        load(j, (SLOTS + j) * CHUNK)

            def body(i, g, then):
                for j in range(SLOTS):
                    slot = (j + SLOTS - 1) % SLOTS
                    if j == 0:
                        load(slot, i * (SLOTS * CHUNK) + slot * CHUNK)
                    elif then is not None:
                        load(slot, then * (SLOTS * CHUNK) + slot * CHUNK)
                    for b, u in units(j, g):
                        sp.wait_ge(evacuated[u % BANKS], uses(i, u, g) + 1)
                        sp.sem_inc(store_asked, 1)
                        store(b, i * (SLOTS * CHUNK) + j * CHUNK, u % BANKS)

            with sp.Fori(1, ROUNDS - 1) as i:
                body(i, 0, i + 1)
            body(ROUNDS - 1, 0, 0)
            with sp.Fori(0, ROUNDS - 1) as i:
                body(i, 1, i + 1)
            body(ROUNDS - 1, 1, None)
            for k in range(BANKS):
                sp.wait_ge(stored[k], 16 * (BLOCKS * CHUNKS // BANKS))

        @block.gpsimd
        def _(pool):
            pool.wait_ge(ident_zeroed, 1)
            pool.affine_select(out=ident[:, :], in_=ident[:, :], compare_op=ALU.not_equal, fill=1.0,
                               base=0, pattern=[[-1, P]], channel_multiplier=1).then_inc(ident_done, 1)
            pool.memset(rows[:, :, :], 0.0).then_inc(rows_zeroed, 1)
            pool.memset(spill_row[:, :], 0.0).then_inc(rows_zeroed, 1)
            pool.wait_ge(rows_zeroed, 2)
            bound = pool.to_reg(LAST - 1)

            def fetch(into, entry, done):
                pool.indirect_dma_start(into, None, items, bass.IndirectOffsetOnAxis(entry, 0),
                                        bounds_check=bound, oob_is_err=False).then_inc(done, 16)

            def fetch_block(b, entries):
                for j in range(FAST):
                    done = j - RING + 3 if j >= RING else j + FAST - RING + 3 - SUM_STEPS
                    if not (isinstance(b, int) and b * SUM_STEPS + done <= 0):
                        pool.wait_ge(sum_step, b * SUM_STEPS + done)
                        pool.sem_inc(fetch_asked, 1)
                    fetch(rows[:, j % RING, :], entries[:, j:j + 1], row_in[j % RING])
                pool.wait_ge(flag_ready, 1)
                spill = pool.value_load(spills[0:1, 0:1], min_val=0, max_val=1)
                with pool.If(spill):
                    with pool.Fori(0, BAG) as c:
                        pool.wait_ge(spill_named, b * BAG + c + 1)
                        pool.sem_inc(fetch_asked, 1)
                        fetch(spill_row[:, :], spill_index[:, 0:1], spill_in)

            pool.wait_ge(sorted_blocks, 1)
            fetch_block(0, index[:, 0, :])
            pool.wait_ge(sorted_blocks, 2)
            fetch_block(1, index[:, 1, :])
            with pool.Fori(1, BLOCKS // 2) as i:
                for half in range(2):
                    b = 2 * i + half
                    pool.tensor_copy(now_index[:, half, :], flat(index)[:, bass.ds(b * FAST, FAST)]).then_inc(index_now, 1)
                    pool.wait_ge(index_now, b - 1)
                    fetch_block(b, now_index[:, half, :])

        @block.scalar
        def _(act):
            def keep_user_part(half):
                for t in range(KT):
                    act.wait_ge(user_done, half * KT + t + 1)
                    nc.scalar.activation(user_part[:, t, half * 512:half * 512 + 512], bank[t][:, :], ACT.Identity,
                                         bias=bf[:, t:t + 1]).then_inc(user_kept, 1)

            def split_hi(slot, use):
                act.wait_ge(w_in[slot], 32 * (use + 1))
                nc.scalar.activation(w_hi[:, slot, :, :], w_raw[:, slot, :, :], ACT.Copy).then_inc(w_hi_done, 1)

            def fuse(b):
                act.wait_ge(bag_turned, b + 1)
                nc.scalar.activation(mean_t[:, :], ps_mean[:, :], ACT.Copy, scale=1.0 / BAG).then_inc(mean_ready, 1)
                act.wait_ge(fused_ready, b + 1)
                nc.scalar.activation(fused_hi[:, :, bass.ds(b * P, P)], fused[:, :, :], ACT.Copy).then_inc(fused_hi_done, 1)

            act.wait_ge(wf_user_in, 32)
            keep_user_part(0)
            split_hi(0, 0)
            for b in range(GROUP):
                fuse(b)
                if b == 0:
                    for slot in range(1, SLOTS):
                        split_hi(slot, 0)
                    keep_user_part(1)
            for slot in range(AHEAD):
                split_hi(slot, 1)

            def body(i, g, ahead=SLOTS):
                for j in range(ahead):
                    split_hi((j + AHEAD) % SLOTS, i + g * ROUNDS + (j + AHEAD) // SLOTS)
                if g == 0:
                    fuse(i + GROUP - 1)

            with act.Fori(1, ROUNDS) as i:
                body(i, 0)
            with act.Fori(0, ROUNDS - 1) as i:
                body(i, 1)
            body(ROUNDS - 1, 1, SLOTS - AHEAD)

        @block.tensor
        def _(pe):
            def user_part_of(half, tiles):
                for t in tiles:
                    if half:
                        pe.wait_ge(evacuated[t], 1)
                    for k in range(KT):
                        mm = nc.tensor.matmul(bank[t][:, :], wf[:, k, t * P:(t + 1) * P],
                                              ut[:, k, half * 512:half * 512 + 512], start=k == 0, stop=k == KT - 1)
                    mm.then_inc(user_done, 1)

            def turn_bag(b):
                pe.wait_ge(sum_step, (b + 1) * SUM_STEPS)
                if not isinstance(b, int) or b:
                    pe.wait_ge(mean_ready, b)
                for t in range(KT):
                    mm = nc.tensor.transpose(ps_mean[:, t * P:(t + 1) * P], bag[:, t * P:(t + 1) * P], ident[:, :])
                mm.then_inc(bag_turned, 1)

            def fuse(b):
                pe.wait_ge(mean_ready, b + 1)
                if not isinstance(b, int) or b:
                    pe.wait_ge(fused_ready, b)
                for t in range(KT):
                    for k in range(KT):
                        mm = nc.tensor.matmul(ps_fused[:, t * P:(t + 1) * P], wf[:, KT + k, t * P:(t + 1) * P],
                                              mean_t[:, k * P:(k + 1) * P], start=k == 0, stop=k == KT - 1)
                mm.then_inc(fuse_done, 1)

            def unit(b, j, k):
                for t in range(KT):
                    hi, lo = fused_hi[:, t, b * P:(b + 1) * P], fused_lo[:, t, b * P:(b + 1) * P]
                    nc.tensor.matmul(bank[k][:, 0:CHUNK], hi, w_hi[:, j, t, :], start=t == 0, stop=False)
                    nc.tensor.matmul(bank[k][:, 0:CHUNK], hi, w_lo[:, j, t, :], start=False, stop=False)
                    mm = nc.tensor.matmul(bank[k][:, 0:CHUNK], lo, w_hi[:, j, t, :], start=False, stop=t == KT - 1)
                mm.then_inc(unit_done, 1)

            pe.wait_ge(wf_user_in, 32)
            pe.wait_ge(users_in[0], 16)
            user_part_of(0, (0, 1))
            pe.wait_ge(rest_flagged, 1)
            pe.wait_ge(ones_done, 1)
            nc.tensor.matmul(ps_flag[0:1, 0:1], rest_any[:, :], ones[:, :], start=True, stop=True).then_inc(flag_summed, 1)
            user_part_of(0, (2, 3))
            pe.wait_ge(ident_done, 1)
            pe.wait_ge(wf_item_in, 16)
            for b in range(GROUP):
                turn_bag(b)
                fuse(b)
                pe.wait_ge(fused_lo_done, b + 1)
                for j in range(SLOTS):
                    if b == 0:
                        pe.wait_ge(w_lo_done, j + 1)
                    else:
                        pe.wait_ge(evacuated[j], b)
                    if b == 1 and j < KT:
                        pe.wait_ge(user_kept, KT + j + 1)
                    unit(b, j, j)
                if b == 0:
                    pe.wait_ge(users_in[1], 16)
                    user_part_of(1, range(KT))

            def body(i, g):
                for j in range(SLOTS):
                    pe.wait_ge(w_lo_done, (i + g * ROUNDS) * SLOTS + j + 1)
                    next_bag = g == 0 and j == SLOTS - 1
                    if next_bag:
                        turn_bag(i + GROUP - 1)
                    for b, u in units(j, g):
                        pe.wait_ge(evacuated[u % BANKS], uses(i, u, g))
                        unit(b, j, u % BANKS)
                        if next_bag and b == 0:
                            fuse(i + GROUP - 1)

            with pe.Fori(1, ROUNDS) as i:
                body(i, 0)
            pe.wait_ge(fused_lo_done, BLOCKS)
            with pe.Fori(0, ROUNDS) as i:
                body(i, 1)

        @block.vector
        def _(dve):
            v = nc.vector
            v.memset(ident[:, :], 0.0).then_inc(ident_zeroed, 1)
            v.memset(ones[:, :], 1.0).then_inc(ones_done, 1)
            steps = [0]

            def step(instruction):
                steps[0] += 1
                instruction.then_inc(sort_step, 1)
                return steps[0]

            def sort(first, end):
                raw, wrapped, keys = raw_index[:, first:end, :], wrap[:, first:end, :], key[:, first:end, :]
                n = step(v.tensor_scalar(wrapped, raw, 0.0, float(V), ALU.is_lt, ALU.mult))
                dve.wait_ge(sort_step, n)
                n = step(v.tensor_tensor(keys, raw, wrapped, ALU.add))
                dve.wait_ge(sort_step, n)
                n = step(v.tensor_scalar(keys, keys, 0.0, float(LAST), ALU.max, ALU.min))
                dve.wait_ge(sort_step, n)
                n = step(v.tensor_scalar(keys, keys, -1.0, None, ALU.mult))
                dve.wait_ge(sort_step, n)
                n = step(v.tensor_scalar(wrapped, keys, -float(LAST), None, ALU.is_equal))
                dve.wait_ge(sort_step, n)
                n = step(v.tensor_reduce(n_last[:, first:end], wrapped, AX.X, ALU.add))
                for e in range(0, FAST, 8):
                    for b in range(first, end):
                        n = step(v.max(top[:, b, e:e + 8], key[:, b, :]))
                    dve.wait_ge(sort_step, n)
                    for b in range(first, end):
                        n = step(v.match_replace(key[:, b, :], top[:, b, e:e + 8], key[:, b, :], REPLACED))
                    dve.wait_ge(sort_step, n)
                tops = top[:, first:end, :]
                v.tensor_scalar(index[:, first:end, :], tops, -1.0, None, ALU.mult).then_inc(sorted_blocks, 1)
                step(v.tensor_scalar(mask[:, first:end, :], tops, -float(LAST), None, ALU.is_gt))
                step(v.tensor_scalar(rest_index[:, first:end, :], keys, -1.0, None, ALU.mult))
                n = step(v.tensor_scalar(rest_mask[:, first:end, :], keys, -float(LAST), None, ALU.is_gt))
                return n

            def sum_start(b):
                if not isinstance(b, int) or b:
                    dve.wait_ge(sum_step, b * SUM_STEPS)
                v.tensor_copy(now_mask[:, :], flat(mask)[:, bass.ds(b * FAST, FAST)]).then_inc(sum_step, 1)
                v.tensor_scalar(acc[:, 0, :], last_row[:, :], n_last[:, bass.ds(b, 1)], None, ALU.mult).then_inc(sum_step, 1)

            def add_row(b, j):
                dve.wait_ge(sum_step, b * SUM_STEPS + 2 + max(0, j - 1))
                dve.wait_ge(row_in[j % RING], 16 * (b * (FAST // RING) + j // RING + 1))
                part, row, m = acc[:, j % ACCS, :], rows[:, j % RING, :], now_mask[:, j:j + 1]
                if j == 1:
                    v.tensor_scalar(part, row, m, None, ALU.mult).then_inc(sum_step, 1)
                else:
                    v.scalar_tensor_tensor(part, row, m, part, ALU.mult, ALU.add).then_inc(sum_step, 1)

            def sum_end(b, spill):
                done = b * SUM_STEPS + 2 + FAST
                with dve.If(spill):
                    with dve.Fori(0, BAG) as c:
                        dve.wait_ge(sum_step, done)
                        before = 3 * (b * BAG + c) + 1
                        dve.wait_ge(spill_added, before)
                        v.tensor_copy(spill_mask[:, :], flat(rest_mask)[:, bass.ds(b * BAG + c, 1)]).then_inc(spill_added, 1)
                        v.tensor_copy(spill_index[:, :], flat(rest_index)[:, bass.ds(b * BAG + c, 1)]).then_inc(spill_named, 1)
                        dve.wait_ge(spill_in, 16 * (b * BAG + c + 1))
                        dve.wait_ge(spill_added, before + 1)
                        v.scalar_tensor_tensor(acc[:, 0, :], spill_row[:, :], spill_mask[:, :], acc[:, 0, :],
                                               ALU.mult, ALU.add).then_inc(spill_added, 2)
                    dve.wait_ge(spill_added, 3 * (b + 1) * BAG + 1)
                    dve.sem_inc(spill_closed, 1)
                dve.wait_ge(sum_step, done)
                if not isinstance(b, int) or b:
                    dve.wait_ge(bag_turned, b)
                v.tensor_tensor(bag[:, :], acc[:, 0, :], acc[:, 1, :], ALU.add).then_inc(sum_step, 1)

            def fuse_add(b):
                dve.wait_ge(fuse_done, b + 1)
                if not isinstance(b, int) or b:
                    dve.wait_ge(fused_hi_done, b)
                    dve.wait_ge(fused_lo_done, b)
                v.tensor_tensor(fused[:, :, :], ps_fused[:, :].rearrange("p (t u) -> p t u", t=KT),
                                user_part[:, :, bass.ds(b * P, P)], ALU.add).then_inc(fused_ready, 1)

            def fuse_lo(b):
                dve.wait_ge(fused_hi_done, b + 1)
                v.tensor_tensor(fused_lo[:, :, bass.ds(b * P, P)], fused[:, :, :],
                                fused_hi[:, :, bass.ds(b * P, P)].bitcast(f32), ALU.subtract).then_inc(fused_lo_done, 1)

            def split_lo(slot, use):
                dve.wait_ge(w_hi_done, use * SLOTS + slot + 1)
                v.tensor_tensor(w_lo[:, slot, :, :], w_raw[:, slot, :, :],
                                w_hi[:, slot, :, :].bitcast(f32), ALU.subtract).then_inc(w_lo_done, 1)

            def evacuate(unit_number, use, slot, k):
                dve.wait_ge(unit_done, unit_number + 1)
                if not isinstance(use, int) or use:
                    dve.wait_ge(stored[k], 16 * use)
                v.tensor_tensor(stage[:, k, :], bank[k][:, 0:CHUNK], bias[:, slot, :], ALU.add).then_inc(evacuated[k], 1)

            dve.sem_inc(spill_added, 1)
            dve.wait_ge(index_in, 16)
            dve.wait_ge(sort_step, sort(0, 1))
            dve.wait_ge(sort_step, sort(1, BLOCKS))
            v.tensor_reduce(rest_any[:, :], rest_mask[:, :, :], AX.XY, ALU.max).then_inc(rest_flagged, 1)

            dve.wait_ge(last_in, 16)
            sum_start(0)
            for j in range(FAST // 2):
                add_row(0, j)
            dve.wait_ge(flag_summed, 1)
            v.tensor_scalar(spills[0:1, 0:1], ps_flag[0:1, 0:1], 1.0, None, ALU.min).then_inc(flag_ready, 1)
            dve.wait_ge(flag_ready, 1)
            spill = dve.value_load(spills[0:1, 0:1], min_val=0, max_val=1)
            for j in range(FAST // 2, FAST):
                add_row(0, j)
            sum_end(0, spill)
            split_lo(0, 0)
            dve.wait_ge(user_kept, KT)
            early = FAST - SLOTS * (FAST // (SLOTS + 1))
            for b in range(GROUP):
                more = b + 1 < GROUP
                if more:
                    sum_start(b + 1)
                    for r in range(early):
                        add_row(b + 1, r)
                fuse_add(b)
                fuse_lo(b)
                for j in range(SLOTS):
                    if b == 0 and j + 1 < SLOTS:
                        split_lo(j + 1, 0)
                    if more:
                        for r in range(FAST // (SLOTS + 1)):
                            add_row(b + 1, early + j * (FAST // (SLOTS + 1)) + r)
                    if not more and j == SLOTS - 2:
                        split_lo(0, 1)
                    evacuate(number(0, b * SLOTS + j, 0), b, j, j)
                if more:
                    sum_end(b + 1, spill)
            for slot in range(1, AHEAD):
                split_lo(slot, 1)

            def body(i, g, ahead=SLOTS):
                b, per = i + GROUP - 1, FAST // (SLOTS - 1)
                for j in range(SLOTS):
                    if j < ahead:
                        split_lo((j + AHEAD) % SLOTS, i + g * ROUNDS + (j + AHEAD) // SLOTS)
                    if g == 0 and j < SLOTS - 1:
                        if j == 0:
                            sum_start(b)
                        for r in range(j * per, (j + 1) * per):
                            add_row(b, r)
                        if j == SLOTS - 2:
                            sum_end(b, spill)
                    for m, (_, u) in enumerate(units(j, g)):
                        evacuate(number(i, u, g), uses(i, u, g), j, u % BANKS)
                        if g == 0 and j == SLOTS - 1 and m == 1:
                            fuse_add(b)
                        if g == 0 and j == SLOTS - 1 and m == 2:
                            fuse_lo(b)

            dve.wait_ge(user_kept, 2 * KT)
            with dve.Fori(1, ROUNDS) as i:
                body(i, 0)
            with dve.Fori(0, ROUNDS - 1) as i:
                body(i, 1)
            body(ROUNDS - 1, 1, SLOTS - AHEAD)


def kernel(r_user_rep, r_indices, L0_rec_item_embeddings, L0_rec_W_fuse, L0_rec_b_fuse, L0_rec_W_proj, L0_rec_b_proj):
    import numpy as np
    import concourse.bacc as bacc
    from concourse.bass_utils import run_bass_kernel_spmd

    nc = bacc.Bacc("TRN2", target_bir_lowering=False, num_devices=1)
    given = {
        "user_t": np.ascontiguousarray(np.asarray(r_user_rep).T),
        "indices": np.ascontiguousarray(r_indices),
        "items": np.ascontiguousarray(L0_rec_item_embeddings),
        "w_fuse": np.ascontiguousarray(L0_rec_W_fuse),
        "b_fuse": np.ascontiguousarray(L0_rec_b_fuse),
        "w_proj": np.ascontiguousarray(L0_rec_W_proj),
        "b_proj": np.ascontiguousarray(L0_rec_b_proj).reshape(1, V),
    }
    args = [nc.dram_tensor(name, a.shape, mybir.dt.from_np(a.dtype), kind="ExternalInput").ap()
            for name, a in given.items()]
    out = nc.dram_tensor("out", (USERS, V), mybir.dt.float32, kind="ExternalOutput").ap()
    program(nc, *args, out)
    got = run_bass_kernel_spmd(nc, [given], core_ids=[0])
    return got.results[0]["out"]
```

```python
import concourse.bass as bass
from concourse import mybir
from contextlib import ExitStack

P = 128
USERS, BAG, H, V = 1024, 50, 512, 12500
BLOCKS = USERS // P
KT = H // P
CHUNK = 500
CHUNKS = V // CHUNK
SLOTS = 5
ROUNDS = CHUNKS // SLOTS
GROUP = BLOCKS // 2
SPLIT_EARLY = 2
PLAIN = 2 * (SLOTS - SPLIT_EARLY)
START = PLAIN + SPLIT_EARLY
FIRST = 2
BANKS = 5
FAST = 24
RING = 8
LAST = V - 1
ACCS = 2
SUM_STEPS = 2 + FAST + 1
AHEAD = 2
START_PLACE = ([((START + n // 2) % SLOTS, n % 2) for n in range(PLAIN)] +
               [(n % SLOTS, 0) for n in range(PLAIN, START)])
BIAS_ORDER = sorted(range(START), key=lambda n: START_PLACE[n][1])
LOAD_AFTER = ((0, 14), (0, 20), (0, 24), (1, 1), (1, 3), (1, 6), (1, 9), (1, 12))
WF_AFTER = (0, 1)
USERS_AFTER = (0, 8)
PER_UNIT, EARLY = (6, 4, 4, 4), (2, 4, 4, 4)
REPLACED = -1.0e9


def program(nc, user_t, indices, items, w_fuse, b_fuse, w_proj, b_proj, out):
    f32, f32r, i32 = mybir.dt.float32, mybir.dt.float32r, mybir.dt.int32
    ALU, ACT, AX = mybir.AluOpType, mybir.ActivationFunctionType, mybir.AxisListType

    w_view = w_proj.rearrange("(t p) n -> p t n", p=P)
    ctx = ExitStack()
    with ctx:
        def sb(name, shape, dt=f32):
            return ctx.enter_context(nc.sbuf_tensor(name, shape, dt))

        def sem(name):
            return ctx.enter_context(nc.semaphore(name))

        chunk_bytes, fused_bytes = KT * CHUNK * 4, KT * USERS * 4
        arena = sb("arena", [P, (SLOTS * chunk_bytes + fused_bytes) // 4])
        at = nc.lookup_mloc(arena).addr
        w_raw = nc.alloc_sbuf_tensor_at("w_raw", [P, SLOTS, KT, CHUNK], f32, offset=at)
        w_lo = nc.alloc_sbuf_tensor_at("w_lo", [P, SLOTS, KT, CHUNK], f32r, offset=at)
        user_part = nc.alloc_sbuf_tensor_at("user_part", [P, KT, USERS], f32, offset=at + SLOTS * chunk_bytes)
        fused_lo = nc.alloc_sbuf_tensor_at("fused_lo", [P, KT, USERS], f32r, offset=at + SLOTS * chunk_bytes)
        w_hi_arena = sb("w_hi_arena", [P, SLOTS * chunk_bytes // 4])
        at_hi = nc.lookup_mloc(w_hi_arena).addr
        w_late = nc.alloc_sbuf_tensor_at("w_late", [P, SLOTS, KT, CHUNK], f32, offset=at_hi)
        w_hi = nc.alloc_sbuf_tensor_at("w_hi", [P, SLOTS, KT, CHUNK], f32r, offset=at_hi)
        fused_hi = sb("fused_hi", [P, KT, USERS], f32r)
        bias = sb("bias", [P, SLOTS, CHUNK])
        bias_rows = sb("bias_rows", [START, CHUNK])
        stage = sb("stage", [P, BANKS, CHUNK])
        rows = sb("rows", [P, RING, H])
        spill_row = sb("spill_row", [P, H])
        acc = sb("acc", [P, ACCS, H])
        bag = sb("bag", [P, H])
        mean_t = sb("mean_t", [P, H])
        fused = sb("fused", [P, 2, KT, P])
        wf = sb("wf", [P, 2 * KT, H])
        bf = sb("bf", [P, KT])
        early_arena = sb("early_arena", [P, 2 * BLOCKS * BAG + KT * USERS])
        at_early, index_bytes = nc.lookup_mloc(early_arena).addr, BLOCKS * BAG * 4
        wrap = nc.alloc_sbuf_tensor_at("wrap", [P, BLOCKS, BAG], f32, offset=at_early)
        raw_index = nc.alloc_sbuf_tensor_at("raw_index", [P, BLOCKS, BAG], i32, offset=at_early + index_bytes)
        ut = nc.alloc_sbuf_tensor_at("ut", [P, 2, KT, 512], f32, offset=at_early + 2 * index_bytes)
        late_bias = nc.alloc_sbuf_tensor_at("late_bias", [P, PLAIN // 2, CHUNK], f32, offset=at_early)
        assert PLAIN // 2 * CHUNK * 4 <= 2 * index_bytes + KT * 512 * 4
        last_row = sb("last_row", [P, H])
        key = sb("key", [P, BLOCKS, BAG])
        top = sb("top", [P, BLOCKS, FAST])
        index = sb("index", [P, BLOCKS, FAST], i32)
        mask = sb("mask", [P, BLOCKS, FAST])
        rest_index = sb("rest_index", [P, BLOCKS, BAG], i32)
        rest_mask = sb("rest_mask", [P, BLOCKS, BAG])
        n_last = sb("n_last", [P, BLOCKS])
        now_index = sb("now_index", [P, 2, FAST], i32)
        now_mask = sb("now_mask", [P, FAST])
        spill_index = sb("spill_index", [P, 1], i32)
        spill_mask = sb("spill_mask", [P, 1])
        rest_any = sb("rest_any", [P, 1])
        ones = sb("ones", [P, 1])
        spills = sb("spills", [1, 1], i32)
        ident = sb("ident", [P, P])

        bank = [ctx.enter_context(nc.psum_tensor(f"bank{n}", [P, 512], f32)) for n in range(8)]
        ps_mean, ps_fused, ps_flag = bank[BANKS], bank[BANKS + 1], bank[BANKS + 2]
        ps_late_users = bank[BANKS + 2]

        index_in, last_in = sem("index_in"), sem("last_in")
        bias_rows_in, bias_spread, bias_kept = sem("bias_rows_in"), sem("bias_spread"), sem("bias_kept")
        wf_user_in, wf_item_in = sem("wf_user_in"), sem("wf_item_in")
        users_in = [sem("users_in0"), sem("users_in1")]
        w_in = [sem(f"w_in{s}") for s in range(SLOTS)]
        w_late_in = [sem(f"w_late_in{s}") for s in range(SLOTS)]
        w_hi_done, w_lo_done = sem("w_hi_done"), sem("w_lo_done")
        row_in = [sem(f"row_in{r}") for r in range(RING)]
        sort_step, sorted_blocks = sem("sort_step"), sem("sorted_blocks")
        sum_step = sem("sum_step")
        ident_zeroed, ident_done, ones_done = sem("ident_zeroed"), sem("ident_done"), sem("ones_done")
        rows_zeroed, index_now = sem("rows_zeroed"), sem("index_now")
        rest_flagged, flag_summed, flag_ready = sem("rest_flagged"), sem("flag_summed"), sem("flag_ready")
        fetch_asked, store_asked, spill_closed = sem("fetch_asked"), sem("store_asked"), sem("spill_closed")
        spill_named, spill_in, spill_added = sem("spill_named"), sem("spill_in"), sem("spill_added")
        user_done, user_kept = sem("user_done"), sem("user_kept")
        bag_turned, mean_ready = sem("bag_turned"), sem("mean_ready")
        fuse_done, fused_ready, fused_hi_done, fused_lo_done = (
            sem("fuse_done"), sem("fused_ready"), sem("fused_hi_done"), sem("fused_lo_done"))
        unit_done = sem("unit_done")
        evacuated = [sem(f"evacuated{k}") for k in range(BANKS)]
        stored = [sem(f"stored{k}") for k in range(BANKS)]

        def added(b, n):
            return b * SUM_STEPS + 2 + n

        per_round = SLOTS * GROUP

        def units(j, g):
            return [(g * GROUP + m, j * GROUP + m) for m in range(GROUP)]

        def number(i, u, g):
            return (g * ROUNDS + i) * per_round + u

        def split(i, slot, g):
            return g * CHUNKS + i * SLOTS + slot - PLAIN + 1

        def landings(i, slot, g):
            return 16 + 32 * (i + g * ROUNDS - (slot < START % SLOTS))

        def uses(i, u, g):
            return (g * ROUNDS + i) * (per_round // BANKS) + u // BANKS

        def flat(t):
            return t[:, :, :].rearrange("p b k -> p (b k)")

        def users_bank(half, t):
            return (ps_late_users if t else ps_fused) if half else bank[t]

        def bias_bank(m):
            return bank[BANKS - 2 + m if m < SLOTS else m - SLOTS]

        def start_bias(n):
            slot, late = START_PLACE[n]
            return late_bias[:, n // 2, :] if late else bias[:, slot, :]

        block = ctx.enter_context(nc.Block())

        @block.sync
        def _(sp):
            def load(slot, chunk_start):
                sp.dma_start(w_raw[:, slot, :, :], w_view[:, :, bass.ds(chunk_start, CHUNK)]).then_inc(w_in[slot], 16)
                sp.dma_start(bias[:, slot, :],
                             b_proj[:, bass.ds(chunk_start, CHUNK)].to_broadcast([P, CHUNK])).then_inc(w_in[slot], 16)

            def load_users(half):
                sp.dma_start(ut[:, half, :, :],
                             user_t.rearrange("(t p) n -> p t n", p=P)[:, :, half * 512:half * 512 + 512]
                             ).then_inc(users_in[half], 16)

            def store(b, chunk_start, k):
                sp.dma_start(out[b * P:(b + 1) * P, bass.ds(chunk_start, CHUNK)], stage[:, k, :]).then_inc(stored[k], 16)

            sp.dma_start(raw_index[:, :, :], indices.rearrange("(b p) k -> p b k", p=P)).then_inc(index_in, 16)
            sp.dma_start(bias_rows[:, :], b_proj[0:1, 0:START * CHUNK].rearrange("a (c n) -> (a c) n", c=START)
                         ).then_inc(bias_rows_in, 16)
            wf_view = w_fuse.rearrange("(t p) n -> p t n", p=P)
            sp.dma_start(wf[:, 0:KT, :], wf_view[:, 0:KT, :]).then_inc(wf_user_in, 16)
            load_users(0)
            sp.dma_start(last_row[:, :], items[LAST:V, :].to_broadcast([P, H])).then_inc(last_in, 16)
            with nc.allow_non_contiguous_dma(reason="512 biases, once"):
                sp.dma_start(bf[:, :], b_fuse.rearrange("(t p) -> p t", p=P)).then_inc(wf_user_in, 16)
            sp.wait_ge(sum_step, added(*WF_AFTER))
            sp.dma_start(wf[:, KT:2 * KT, :], wf_view[:, KT:2 * KT, :]).then_inc(wf_item_in, 16)
            sp.wait_ge(sum_step, added(*USERS_AFTER))
            load_users(1)

            def load_start(n):
                sp.wait_ge(sum_step, added(*LOAD_AFTER[n]))
                slot, late = START_PLACE[n]
                into, landed = (w_late, w_late_in) if late else (w_raw, w_in)
                sp.dma_start(into[:, slot, :, :], w_view[:, :, n * CHUNK:(n + 1) * CHUNK]).then_inc(landed[slot], 16)

            for n in range(SLOTS):
                load_start(n)
            for b in range(GROUP):
                for n in range(START):
                    u = b * START + n
                    sp.wait_ge(evacuated[u % BANKS], uses(0, u, 0) + 1)
                    store(b, n * CHUNK, u % BANKS)
                    if b == 0 and SLOTS + n < START:
                        load_start(SLOTS + n)
                    slot, late = START_PLACE[n]
                    if b == GROUP - 1 and (late or n >= PLAIN) and n < START - 1:
                        load(slot, (START + (slot - START) % SLOTS) * CHUNK)

            def body(i, g, then, first=0):
                for j in range(first, SLOTS):
                    slot = (j + SLOTS - 1) % SLOTS
                    if j == 0:
                        load(slot, i * (SLOTS * CHUNK) + slot * CHUNK)
                    elif then is not None:
                        load(slot, then * (SLOTS * CHUNK) + slot * CHUNK)
                    for b, u in units(j, g):
                        sp.wait_ge(evacuated[u % BANKS], uses(i, u, g) + 1)
                        sp.sem_inc(store_asked, 1)
                        store(b, i * (SLOTS * CHUNK) + j * CHUNK, u % BANKS)

            body(FIRST - 1, 0, FIRST, START % SLOTS)
            with sp.Fori(FIRST, ROUNDS - 1) as i:
                body(i, 0, i + 1)
            body(ROUNDS - 1, 0, 0)
            with sp.Fori(0, ROUNDS - 1) as i:
                body(i, 1, i + 1)
            body(ROUNDS - 1, 1, None)
            for k in range(BANKS):
                sp.wait_ge(stored[k], 16 * (BLOCKS * CHUNKS // BANKS))

        @block.gpsimd
        def _(pool):
            pool.wait_ge(ident_zeroed, 1)
            pool.affine_select(out=ident[:, :], in_=ident[:, :], compare_op=ALU.not_equal, fill=1.0,
                               base=0, pattern=[[-1, P]], channel_multiplier=1).then_inc(ident_done, 1)
            pool.memset(rows[:, :, :], 0.0).then_inc(rows_zeroed, 1)
            pool.memset(spill_row[:, :], 0.0).then_inc(rows_zeroed, 1)
            pool.wait_ge(rows_zeroed, 2)
            bound = pool.to_reg(LAST - 1)

            def fetch(into, entry, done):
                pool.indirect_dma_start(into, None, items, bass.IndirectOffsetOnAxis(entry, 0),
                                        bounds_check=bound, oob_is_err=False).then_inc(done, 16)

            def fetch_block(b, entries):
                for j in range(FAST):
                    done = j - RING + 3 if j >= RING else j + FAST - RING + 3 - SUM_STEPS
                    if not (isinstance(b, int) and b * SUM_STEPS + done <= 0):
                        pool.wait_ge(sum_step, b * SUM_STEPS + done)
                        pool.sem_inc(fetch_asked, 1)
                    fetch(rows[:, j % RING, :], entries[:, j:j + 1], row_in[j % RING])
                pool.wait_ge(flag_ready, 1)
                spill = pool.value_load(spills[0:1, 0:1], min_val=0, max_val=1)
                with pool.If(spill):
                    with pool.Fori(0, BAG) as c:
                        pool.wait_ge(spill_named, b * BAG + c + 1)
                        pool.sem_inc(fetch_asked, 1)
                        fetch(spill_row[:, :], spill_index[:, 0:1], spill_in)

            pool.wait_ge(sorted_blocks, 1)
            fetch_block(0, index[:, 0, :])
            pool.wait_ge(sorted_blocks, 2)
            fetch_block(1, index[:, 1, :])
            pool.wait_ge(sorted_blocks, 3)
            with pool.Fori(1, BLOCKS // 2) as i:
                for half in range(2):
                    b = 2 * i + half
                    pool.tensor_copy(now_index[:, half, :], flat(index)[:, bass.ds(b * FAST, FAST)]).then_inc(index_now, 1)
                    pool.wait_ge(index_now, b - 1)
                    fetch_block(b, now_index[:, half, :])

        @block.scalar
        def _(act):
            def keep_user_part(half, first=0, end=KT):
                for t in range(first, end):
                    act.wait_ge(user_done, half * KT + t + 1)
                    nc.scalar.activation(user_part[:, t, half * 512:half * 512 + 512], users_bank(half, t)[:, :],
                                         ACT.Identity, bias=bf[:, t:t + 1]).then_inc(user_kept, 1)

            def keep_biases(first, end):
                for m in range(first, end):
                    act.wait_ge(bias_spread, m + 1)
                    nc.scalar.activation(start_bias(BIAS_ORDER[m]), bias_bank(m)[:, 0:CHUNK], ACT.Copy).then_inc(bias_kept, 1)

            def split_hi(i, slot, g):
                act.wait_ge(w_in[slot], landings(i, slot, g))
                nc.scalar.activation(w_hi[:, slot, :, :], w_raw[:, slot, :, :], ACT.Copy).then_inc(w_hi_done, 1)

            def keep_means(b):
                act.wait_ge(bag_turned, b + 1)
                nc.scalar.activation(mean_t[:, :], ps_mean[:, :], ACT.Copy, scale=1.0 / BAG).then_inc(mean_ready, 1)

            def fuse_hi(b, buffer):
                act.wait_ge(fused_ready, b + 1)
                nc.scalar.activation(fused_hi[:, :, bass.ds(b * P, P)], fused[:, buffer, :, :], ACT.Copy).then_inc(fused_hi_done, 1)

            keep_biases(0, SLOTS)
            act.wait_ge(wf_user_in, 32)
            keep_user_part(0)
            act.wait_ge(sorted_blocks, 3)
            keep_biases(SLOTS, START)
            keep_user_part(1, 0, 1)
            keep_means(0)
            keep_user_part(1, 1, 2)
            fuse_hi(0, 0)
            keep_user_part(1, 2, KT)
            for n in range(PLAIN, START):
                split_hi(n // SLOTS, n % SLOTS, 0)
            for b in range(1, GROUP):
                keep_means(b)
                fuse_hi(b, b % 2)
            for n in range(START, START + AHEAD):
                split_hi(n // SLOTS, n % SLOTS, 0)

            def body(i, g, first=0, ahead=SLOTS):
                b = i + BLOCKS - ROUNDS
                for j in range(first, ahead):
                    if g == 0 and j == SLOTS - 1:
                        keep_means(b)
                    split_hi(i + (j + AHEAD) // SLOTS, (j + AHEAD) % SLOTS, g)
                if g == 0:
                    fuse_hi(b, 0)

            body(FIRST - 1, 0, START % SLOTS)
            with act.Fori(FIRST, ROUNDS) as i:
                body(i, 0)
            with act.Fori(0, ROUNDS - 1) as i:
                body(i, 1)
            body(ROUNDS - 1, 1, 0, SLOTS - AHEAD)

        @block.tensor
        def _(pe):
            def spread_biases(first, end):
                for m in range(first, end):
                    if m >= SLOTS:
                        pe.wait_ge(user_kept, m - SLOTS + 1)
                    pick = ident[0:START, BIAS_ORDER[m]:BIAS_ORDER[m] + 1].to_broadcast([START, P])
                    nc.tensor.matmul(bias_bank(m)[:, 0:CHUNK], pick, bias_rows[:, :],
                                     start=True, stop=True).then_inc(bias_spread, 1)

            def users_tile(half, t):
                if half and t == 0:
                    pe.wait_ge(users_in[1], 16)
                    pe.wait_ge(bias_kept, 4)
                elif half and t == 1:
                    pe.wait_ge(flag_ready, 1)
                elif half:
                    pe.wait_ge(user_kept, KT + t)
                for k in range(KT):
                    mm = nc.tensor.matmul(users_bank(half, t)[:, :], wf[:, k, t * P:(t + 1) * P],
                                          ut[:, half, k, :], start=k == 0, stop=k == KT - 1)
                mm.then_inc(user_done, 1)

            def turn_bag(b):
                pe.wait_ge(sum_step, (b + 1) * SUM_STEPS)
                if not isinstance(b, int) or b:
                    pe.wait_ge(mean_ready, b)
                for t in range(KT):
                    mm = nc.tensor.transpose(ps_mean[:, t * P:(t + 1) * P], bag[:, t * P:(t + 1) * P], ident[:, :])
                mm.then_inc(bag_turned, 1)

            def fuse(b):
                pe.wait_ge(mean_ready, b + 1)
                if not isinstance(b, int) or b:
                    pe.wait_ge(fused_ready, b)
                for t in range(KT):
                    for k in range(KT):
                        mm = nc.tensor.matmul(ps_fused[:, t * P:(t + 1) * P], wf[:, KT + k, t * P:(t + 1) * P],
                                              mean_t[:, k * P:(k + 1) * P], start=k == 0, stop=k == KT - 1)
                mm.then_inc(fuse_done, 1)

            def plain_unit(b, n, k):
                slot, late = START_PLACE[n]
                weights = w_late if late else w_raw
                for t in range(KT):
                    mm = nc.tensor.matmul(bank[k][:, 0:CHUNK], fused[:, b % 2, t, :], weights[:, slot, t, :],
                                          start=t == 0, stop=t == KT - 1)
                mm.then_inc(unit_done, 1)

            def unit(b, j, k):
                for t in range(KT):
                    hi, lo = fused_hi[:, t, b * P:(b + 1) * P], fused_lo[:, t, b * P:(b + 1) * P]
                    nc.tensor.matmul(bank[k][:, 0:CHUNK], hi, w_hi[:, j, t, :], start=t == 0, stop=False)
                    nc.tensor.matmul(bank[k][:, 0:CHUNK], hi, w_lo[:, j, t, :], start=False, stop=False)
                    mm = nc.tensor.matmul(bank[k][:, 0:CHUNK], lo, w_hi[:, j, t, :], start=False, stop=t == KT - 1)
                mm.then_inc(unit_done, 1)

            pe.wait_ge(bias_rows_in, 16)
            pe.wait_ge(ident_done, 1)
            spread_biases(0, SLOTS)
            pe.wait_ge(wf_user_in, 32)
            pe.wait_ge(users_in[0], 16)
            for t in range(KT):
                if t == BANKS - 2:
                    pe.wait_ge(bias_kept, 1)
                users_tile(0, t)
            spread_biases(SLOTS, START)
            pe.wait_ge(rest_flagged, 1)
            pe.wait_ge(ones_done, 1)
            nc.tensor.matmul(ps_flag[0:1, 0:1], rest_any[:, :], ones[:, :], start=True, stop=True).then_inc(flag_summed, 1)
            users_tile(1, 0)
            pe.wait_ge(wf_item_in, 16)
            turn_bag(0)
            users_tile(1, 1)
            fuse(0)
            users_tile(1, 2)
            for b in range(GROUP):
                pe.wait_ge(fused_ready, b + 1)
                for n in range(START):
                    if b < GROUP - 1 and n == START - 2:
                        turn_bag(b + 1)
                    if b < GROUP - 1 and n == START - 1:
                        fuse(b + 1)
                    u = b * START + n
                    k, (slot, late) = u % BANKS, START_PLACE[n]
                    if n >= PLAIN:
                        pe.wait_ge(w_lo_done, n - PLAIN + 1)
                        pe.wait_ge(fused_lo_done, b + 1)
                    elif b == 0:
                        pe.wait_ge((w_late_in if late else w_in)[slot], 16)
                    if u >= BANKS:
                        pe.wait_ge(evacuated[k], uses(0, u, 0))
                    if n < PLAIN:
                        plain_unit(b, n, k)
                    else:
                        unit(b, slot, k)
                    if u == 0:
                        users_tile(1, 3)

            def body(i, g, first=0):
                for j in range(first, SLOTS):
                    pe.wait_ge(w_lo_done, split(i, j, g))
                    next_bag = g == 0 and j == SLOTS - 1
                    if next_bag:
                        turn_bag(i + BLOCKS - ROUNDS)
                    for b, u in units(j, g):
                        pe.wait_ge(evacuated[u % BANKS], uses(i, u, g))
                        unit(b, j, u % BANKS)
                        if next_bag and b == 0:
                            fuse(i + BLOCKS - ROUNDS)

            body(FIRST - 1, 0, START % SLOTS)
            with pe.Fori(FIRST, ROUNDS) as i:
                body(i, 0)
            pe.wait_ge(fused_lo_done, BLOCKS)
            with pe.Fori(0, ROUNDS) as i:
                body(i, 1)

        @block.vector
        def _(dve):
            v = nc.vector
            v.memset(ident[:, :], 0.0).then_inc(ident_zeroed, 1)
            v.memset(ones[:, :], 1.0).then_inc(ones_done, 1)
            steps = [0]

            def step(instruction):
                steps[0] += 1
                instruction.then_inc(sort_step, 1)
                return steps[0]

            def make_keys(first, end):
                raw, wrapped, keys = raw_index[:, first:end, :], wrap[:, first:end, :], key[:, first:end, :]
                n = step(v.tensor_scalar(wrapped, raw, 0.0, float(V), ALU.is_lt, ALU.mult))
                dve.wait_ge(sort_step, n)
                n = step(v.tensor_tensor(keys, raw, wrapped, ALU.add))
                dve.wait_ge(sort_step, n)
                n = step(v.tensor_scalar(keys, keys, 0.0, float(LAST), ALU.max, ALU.min))
                dve.wait_ge(sort_step, n)
                n = step(v.tensor_scalar(keys, keys, -1.0, None, ALU.mult))
                dve.wait_ge(sort_step, n)
                n = step(v.tensor_scalar(wrapped, keys, -float(LAST), None, ALU.is_equal))
                dve.wait_ge(sort_step, n)
                step(v.tensor_reduce(n_last[:, first:end], wrapped, AX.X, ALU.add))

            def take_eight(first, end, e):
                dve.wait_ge(sort_step, steps[0])
                for b in range(first, end):
                    n = step(v.max(top[:, b, e:e + 8], key[:, b, :]))
                dve.wait_ge(sort_step, n)
                for b in range(first, end):
                    step(v.match_replace(key[:, b, :], top[:, b, e:e + 8], key[:, b, :], REPLACED))

            def name_entries(first, end):
                dve.wait_ge(sort_step, steps[0])
                keys, tops = key[:, first:end, :], top[:, first:end, :]
                v.tensor_scalar(index[:, first:end, :], tops, -1.0, None, ALU.mult).then_inc(sorted_blocks, 1)
                step(v.tensor_scalar(mask[:, first:end, :], tops, -float(LAST), None, ALU.is_gt))
                step(v.tensor_scalar(rest_index[:, first:end, :], keys, -1.0, None, ALU.mult))
                step(v.tensor_scalar(rest_mask[:, first:end, :], keys, -float(LAST), None, ALU.is_gt))

            def sum_start(b):
                if not isinstance(b, int) or b:
                    dve.wait_ge(sum_step, b * SUM_STEPS)
                v.tensor_copy(now_mask[:, :], flat(mask)[:, bass.ds(b * FAST, FAST)]).then_inc(sum_step, 1)
                v.tensor_scalar(acc[:, 0, :], last_row[:, :], n_last[:, bass.ds(b, 1)], None, ALU.mult).then_inc(sum_step, 1)

            def add_row(b, j):
                dve.wait_ge(sum_step, b * SUM_STEPS + 2 + max(0, j - 1))
                dve.wait_ge(row_in[j % RING], 16 * (b * (FAST // RING) + j // RING + 1))
                part, row, m = acc[:, j % ACCS, :], rows[:, j % RING, :], now_mask[:, j:j + 1]
                if j == 1:
                    v.tensor_scalar(part, row, m, None, ALU.mult).then_inc(sum_step, 1)
                else:
                    v.scalar_tensor_tensor(part, row, m, part, ALU.mult, ALU.add).then_inc(sum_step, 1)

            def sum_end(b, spill):
                done = b * SUM_STEPS + 2 + FAST
                with dve.If(spill):
                    with dve.Fori(0, BAG) as c:
                        dve.wait_ge(sum_step, done)
                        before = 3 * (b * BAG + c) + 1
                        dve.wait_ge(spill_added, before)
                        v.tensor_copy(spill_mask[:, :], flat(rest_mask)[:, bass.ds(b * BAG + c, 1)]).then_inc(spill_added, 1)
                        v.tensor_copy(spill_index[:, :], flat(rest_index)[:, bass.ds(b * BAG + c, 1)]).then_inc(spill_named, 1)
                        dve.wait_ge(spill_in, 16 * (b * BAG + c + 1))
                        dve.wait_ge(spill_added, before + 1)
                        v.scalar_tensor_tensor(acc[:, 0, :], spill_row[:, :], spill_mask[:, :], acc[:, 0, :],
                                               ALU.mult, ALU.add).then_inc(spill_added, 2)
                    dve.wait_ge(spill_added, 3 * (b + 1) * BAG + 1)
                    dve.sem_inc(spill_closed, 1)
                dve.wait_ge(sum_step, done)
                if not isinstance(b, int) or b:
                    dve.wait_ge(bag_turned, b)
                v.tensor_tensor(bag[:, :], acc[:, 0, :], acc[:, 1, :], ALU.add).then_inc(sum_step, 1)

            def fuse_add(b, buffer):
                dve.wait_ge(fuse_done, b + 1)
                if not isinstance(b, int) or b:
                    dve.wait_ge(fused_hi_done, b)
                    dve.wait_ge(fused_lo_done, b)
                v.tensor_tensor(fused[:, buffer, :, :], ps_fused[:, :].rearrange("p (t u) -> p t u", t=KT),
                                user_part[:, :, bass.ds(b * P, P)], ALU.add).then_inc(fused_ready, 1)

            def fuse_lo(b, buffer):
                dve.wait_ge(fused_hi_done, b + 1)
                v.tensor_tensor(fused_lo[:, :, bass.ds(b * P, P)], fused[:, buffer, :, :],
                                fused_hi[:, :, bass.ds(b * P, P)].bitcast(f32), ALU.subtract).then_inc(fused_lo_done, 1)

            def split_lo(i, slot, g):
                dve.wait_ge(w_hi_done, split(i, slot, g))
                v.tensor_tensor(w_lo[:, slot, :, :], w_raw[:, slot, :, :],
                                w_hi[:, slot, :, :].bitcast(f32), ALU.subtract).then_inc(w_lo_done, 1)

            def evacuate(unit_number, use, biases, k):
                dve.wait_ge(unit_done, unit_number + 1)
                if not isinstance(use, int) or use:
                    dve.wait_ge(stored[k], 16 * use)
                v.tensor_tensor(stage[:, k, :], bank[k][:, 0:CHUNK], biases, ALU.add).then_inc(evacuated[k], 1)

            dve.sem_inc(spill_added, 1)
            dve.wait_ge(index_in, 16)
            for first, end in ((0, 1), (1, BLOCKS // 2)):
                make_keys(first, end)
                for e in range(0, FAST, 8):
                    take_eight(first, end, e)
                name_entries(first, end)
            dve.wait_ge(sort_step, steps[0])
            dve.wait_ge(last_in, 16)
            sum_start(0)
            for j in range(FAST):
                add_row(0, j)
                if j == 1:
                    make_keys(BLOCKS // 2, BLOCKS)
                elif j in (4, 7, 10):
                    take_eight(BLOCKS // 2, BLOCKS, (j - 4) // 3 * 8)
                elif j == 12:
                    name_entries(BLOCKS // 2, BLOCKS)
                elif j == 13:
                    dve.wait_ge(sort_step, steps[0])
                    v.tensor_reduce(rest_any[:, :], rest_mask[:, :, :], AX.XY, ALU.max).then_inc(rest_flagged, 1)
                elif j == 18:
                    dve.wait_ge(flag_summed, 1)
                    v.tensor_scalar(spills[0:1, 0:1], ps_flag[0:1, 0:1], 1.0, None, ALU.min).then_inc(flag_ready, 1)
                    dve.wait_ge(flag_ready, 1)
                    spill = dve.value_load(spills[0:1, 0:1], min_val=0, max_val=1)
            sum_end(0, spill)
            sum_start(1)
            for r in range(EARLY[0]):
                add_row(1, r)
            dve.wait_ge(bias_kept, START)
            fuse_add(0, 0)
            for b in range(GROUP):
                for n in range(START):
                    if n < START - 2:
                        begin = EARLY[b] + n * PER_UNIT[b]
                        for r in range(begin, min(FAST, begin + PER_UNIT[b])):
                            add_row(b + 1, r)
                            if r == FAST - 1:
                                sum_end(b + 1, spill)
                    elif b < GROUP - 1:
                        early, part = EARLY[b + 1], n - (START - 2)
                        if part == 0:
                            sum_start(b + 2)
                        for r in range(part * early // 2, (part + 1) * early // 2):
                            add_row(b + 2, r)
                        if part == 1:
                            fuse_add(b + 1, (b + 1) % 2)
                    if b == 0 and PLAIN <= n + 1 < START:
                        split_lo((n + 1) // SLOTS, (n + 1) % SLOTS, 0)
                    u = b * START + n
                    evacuate(u, uses(0, u, 0), start_bias(n), u % BANKS)
                    if n == 0:
                        fuse_lo(b, b % 2)
                    if b == GROUP - 1 and n == START - 3:
                        split_lo(START // SLOTS, START % SLOTS, 0)
            for n in range(START + 1, START + AHEAD):
                split_lo(n // SLOTS, n % SLOTS, 0)
            dve.wait_ge(user_kept, 2 * KT)

            def body(i, g, first=0, ahead=SLOTS):
                b, per = i + BLOCKS - ROUNDS, FAST // (SLOTS - 1)
                for j in range(first, SLOTS):
                    if j < ahead:
                        split_lo(i + (j + AHEAD) // SLOTS, (j + AHEAD) % SLOTS, g)
                    if g == 0 and first == 0 and j < SLOTS - 1:
                        if j == 0:
                            sum_start(b)
                        for r in range(j * per, (j + 1) * per):
                            add_row(b, r)
                        if j == SLOTS - 2:
                            sum_end(b, spill)
                    for m, (_, u) in enumerate(units(j, g)):
                        evacuate(number(i, u, g), uses(i, u, g), bias[:, j, :], u % BANKS)
                        if g == 0 and j == SLOTS - 1 and m == 1:
                            fuse_add(b, 0)
                        if g == 0 and j == SLOTS - 1 and m == 2:
                            fuse_lo(b, 0)

            body(FIRST - 1, 0, START % SLOTS)
            with dve.Fori(FIRST, ROUNDS) as i:
                body(i, 0)
            with dve.Fori(0, ROUNDS - 1) as i:
                body(i, 1)
            body(ROUNDS - 1, 1, 0, SLOTS - AHEAD)


def kernel(r_user_rep, r_indices, L0_rec_item_embeddings, L0_rec_W_fuse, L0_rec_b_fuse, L0_rec_W_proj, L0_rec_b_proj):
    import numpy as np
    import concourse.bacc as bacc
    from concourse.bass_utils import run_bass_kernel_spmd

    nc = bacc.Bacc("TRN2", target_bir_lowering=False, num_devices=1)
    given = {
        "user_t": np.ascontiguousarray(np.asarray(r_user_rep).T),
        "indices": np.ascontiguousarray(r_indices),
        "items": np.ascontiguousarray(L0_rec_item_embeddings),
        "w_fuse": np.ascontiguousarray(L0_rec_W_fuse),
        "b_fuse": np.ascontiguousarray(L0_rec_b_fuse),
        "w_proj": np.ascontiguousarray(L0_rec_W_proj),
        "b_proj": np.ascontiguousarray(L0_rec_b_proj).reshape(1, V),
    }
    args = [nc.dram_tensor(name, a.shape, mybir.dt.from_np(a.dtype), kind="ExternalInput").ap()
            for name, a in given.items()]
    out = nc.dram_tensor("out", (USERS, V), mybir.dt.float32, kind="ExternalOutput").ap()
    program(nc, *args, out)
    got = run_bass_kernel_spmd(nc, [given], core_ids=[0])
    return got.results[0]["out"]
```
